# Optimizing a Trainium2 kernel written in Bass

```python
import numpy as np
import jax
import jax.numpy as jnp

def _softmax(x, axis=-1):
    return jax.nn.softmax(x, axis=axis)

def _gelu(x):
    return jax.nn.gelu(x, approximate=True)

def _silu(x):
    return jax.nn.silu(x)

def _sigmoid(x):
    return jax.nn.sigmoid(x)

def _layernorm(x, axis=-1, eps=1e-05):
    m = jnp.mean(x, axis=axis, keepdims=True)
    v = jnp.var(x, axis=axis, keepdims=True)
    return (x - m) / jnp.sqrt(v + eps)

def _scatter_add(tgt, idx, src, axis=0):
    return tgt.at[idx].add(src)

def _segment_sum(src, seg, n):
    return jax.ops.segment_sum(src, seg, n)
kernel_name = 'mk_flamingo_gated_d1_seqx_r4_706bae'

def setup_inputs(seed: int=0):
    np.random.seed(seed)
    _w = jnp.asarray

    def _rec_inputs():
        import jax
        import jax.numpy as jnp
        _rk = jax.random.key(seed)
        x = 0.000341 + 1 * jax.random.normal(jax.random.fold_in(_rk, 1), (16, 256, 512), jnp.float32)
        _lenS = 256 - jax.random.randint(jax.random.fold_in(_rk, 7), (16,), 0, max(1, 256 // 4) + 1, jnp.int32)
        _lenS2 = 256 - jax.random.randint(jax.random.fold_in(_rk, 8), (16,), 0, max(1, 256 // 4) + 1, jnp.int32)
        _ctx_2048P = jax.random.normal(jax.random.fold_in(_rk, 11), (16, 16, 512), jnp.float32)
        _ctx_2048c = jax.random.dirichlet(jax.random.fold_in(_rk, 511), 0.3 * jnp.ones((16,), jnp.float32), (16, 256))
        _ctx_2048t = jnp.einsum('bsk,bkd->bsd', _ctx_2048c, _ctx_2048P)
        _ctx_2048t = _ctx_2048t * jax.lax.rsqrt(jnp.mean(jnp.square(_ctx_2048t)) + 1e-12) * 0.953939
        ctx_2048 = -1.47943e-05 + 1.00017 * (_ctx_2048t + 0.3 * jax.random.normal(jax.random.fold_in(_rk, 611), (16, 256, 512), jnp.float32))
        _g = jax.random.normal(jax.random.fold_in(_rk, 9001), (2, 1), jnp.float32)
        _g = jnp.sign(_g) * jnp.maximum(jnp.abs(_g), 1.0) + (_g == 0) * 1.0
        g_xattn = _g[0]
        g_ffn = _g[1]
        return (x, ctx_2048, g_xattn, g_ffn)
    x, ctx_2048, g_xattn, g_ffn = _rec_inputs()

    def _L0_xattn_setup():
        import jax, jax.numpy as jnp
        import numpy as np

        def _wkv(time_decay, time_first, k, v):
            w = -jnp.exp(time_decay)
            u = time_first
            B, T, C = k.shape
            aa = jnp.zeros((B, C), dtype=k.dtype)
            bb = jnp.zeros((B, C), dtype=k.dtype)
            pp = jnp.full((B, C), -1e+38, dtype=k.dtype)

            def step(carry, kv_t):
                aa, bb, pp = carry
                kt, vt = kv_t
                ww = u + kt
                q = jnp.maximum(pp, ww)
                e1 = jnp.exp(pp - q)
                e2 = jnp.exp(ww - q)
                y_t = (e1 * aa + e2 * vt) / (e1 * bb + e2)
                ww2 = pp + w
                q2 = jnp.maximum(ww2, kt)
                e1b = jnp.exp(ww2 - q2)
                e2b = jnp.exp(kt - q2)
                new_carry = (e1b * aa + e2b * vt, e1b * bb + e2b, q2)
                return (new_carry, y_t)
            ks = jnp.transpose(k, (1, 0, 2))
            vs = jnp.transpose(v, (1, 0, 2))
            _, ys = jax.lax.scan(step, (aa, bb, pp), (ks, vs))
            return jnp.transpose(ys, (1, 0, 2))
        key = jax.random.key(seed)
        k1, k2, k3, k4 = jax.random.split(key, 4)
        B, T, C = (8, 256, 512)
        return {'batch_size': B, 'seq_len': T, 'embedding_dim': C, 'time_decay': jax.random.normal(k1, (C,), dtype=jnp.float32), 'time_first': jax.random.normal(k2, (C,), dtype=jnp.float32), 'k': jax.random.normal(k3, (B, T, C), dtype=jnp.float32), 'v': jax.random.normal(k4, (B, T, C), dtype=jnp.float32)}
    _L0_xattn_all = _L0_xattn_setup()
    _L0_xattn_in = {k: v for k, v in _L0_xattn_all.items() if k in ('time_decay', 'time_first')}
    del _L0_xattn_all

    def _L0_ffn_setup():
        import jax, jax.numpy as jnp
        import numpy as np
        B, S, D, H = (4, 512, 512, 2048)

        def fwht(x):
            orig_shape = x.shape
            n = orig_shape[-1]
            x = x.reshape(-1, n)
            h = 1
            while h < n:
                xb = x.reshape(-1, n // (2 * h), 2, h)
                a = xb[:, :, 0, :]
                b = xb[:, :, 1, :]
                x = jnp.stack([a + b, a - b], axis=2).reshape(-1, n)
                h *= 2
            scale = jnp.asarray(1.0 / np.sqrt(n), dtype=x.dtype)
            return (x * scale).reshape(orig_shape)
        key = jax.random.key(seed)
        kx, k1, k2, k3 = jax.random.split(key, 4)
        x = jax.random.normal(kx, (B, S, D), dtype=jnp.float32)
        W1 = jax.random.normal(k1, (H, D), dtype=jnp.float32) * (1.0 / np.sqrt(D))
        W2 = jax.random.normal(k2, (D, H), dtype=jnp.float32) * (1.0 / np.sqrt(H))
        W3 = jax.random.normal(k3, (H, D), dtype=jnp.float32) * (1.0 / np.sqrt(D))
        return {'x': x, 'W1': W1, 'W2': W2, 'W3': W3}
    _L0_ffn_all = _L0_ffn_setup()
    _L0_ffn_in = {k: v for k, v in _L0_ffn_all.items() if k in ('W1', 'W2', 'W3')}
    del _L0_ffn_all
    return {'x': x, 'ctx_2048': ctx_2048, 'g_xattn': g_xattn, 'g_ffn': g_ffn, 'L0_xattn_time_decay': _L0_xattn_in['time_decay'], 'L0_xattn_time_first': _L0_xattn_in['time_first'], 'L0_ffn_W1': _L0_ffn_in['W1'], 'L0_ffn_W2': _L0_ffn_in['W2'], 'L0_ffn_W3': _L0_ffn_in['W3']}

def reference(x, ctx_2048, g_xattn, g_ffn, L0_xattn_time_decay, L0_xattn_time_first, L0_ffn_W1, L0_ffn_W2, L0_ffn_W3):
    import jax
    import jax.numpy as jnp

    def _L0_xattn_ref(batch_size, seq_len, embedding_dim, time_decay, time_first, k, v):
        import jax, jax.numpy as jnp
        import numpy as np

        def _wkv(time_decay, time_first, k, v):
            w = -jnp.exp(time_decay)
            u = time_first
            B, T, C = k.shape
            aa = jnp.zeros((B, C), dtype=k.dtype)
            bb = jnp.zeros((B, C), dtype=k.dtype)
            pp = jnp.full((B, C), -1e+38, dtype=k.dtype)

            def step(carry, kv_t):
                aa, bb, pp = carry
                kt, vt = kv_t
                ww = u + kt
                q = jnp.maximum(pp, ww)
                e1 = jnp.exp(pp - q)
                e2 = jnp.exp(ww - q)
                y_t = (e1 * aa + e2 * vt) / (e1 * bb + e2)
                ww2 = pp + w
                q2 = jnp.maximum(ww2, kt)
                e1b = jnp.exp(ww2 - q2)
                e2b = jnp.exp(kt - q2)
                new_carry = (e1b * aa + e2b * vt, e1b * bb + e2b, q2)
                return (new_carry, y_t)
            ks = jnp.transpose(k, (1, 0, 2))
            vs = jnp.transpose(v, (1, 0, 2))
            _, ys = jax.lax.scan(step, (aa, bb, pp), (ks, vs))
            return jnp.transpose(ys, (1, 0, 2))
        assert seq_len <= 256
        return _wkv(time_decay, time_first, k, v)

    def _L0_ffn_ref(x, W1, W2, W3):
        import jax, jax.numpy as jnp
        import numpy as np
        B, S, D, H = (4, 512, 512, 2048)

        def fwht(x):
            orig_shape = x.shape
            n = orig_shape[-1]
            x = x.reshape(-1, n)
            h = 1
            while h < n:
                xb = x.reshape(-1, n // (2 * h), 2, h)
                a = xb[:, :, 0, :]
                b = xb[:, :, 1, :]
                x = jnp.stack([a + b, a - b], axis=2).reshape(-1, n)
                h *= 2
            scale = jnp.asarray(1.0 / np.sqrt(n), dtype=x.dtype)
            return (x * scale).reshape(orig_shape)
        up_gate = jnp.einsum('bsd,hd->bsh', x, W1)
        up_lin = jnp.einsum('bsd,hd->bsh', x, W3)
        hidden = jax.nn.silu(up_gate) * up_lin
        hidden = fwht(hidden)
        out = jnp.einsum('bsh,dh->bsd', hidden, W2)
        return out
    x = x + jnp.tanh(g_xattn[0]) * _L0_xattn_ref(16, 256, 512, L0_xattn_time_decay, L0_xattn_time_first, _layernorm(x, axis=-1), ctx_2048)
    x = x + jnp.tanh(g_ffn[0]) * _L0_ffn_ref(_layernorm(x, axis=-1), L0_ffn_W1, L0_ffn_W2, L0_ffn_W3)
    return x

_drawn_inputs = setup_inputs


def setup_inputs(seed=0):
    import zlib

    import numpy as np

    out = dict(_drawn_inputs(seed))
    spreads = {}
    factors = {}
    for name, (base, spread) in spreads.items():
        noise = np.random.default_rng([zlib.crc32(name.encode()), seed]).standard_normal(out[name].shape)
        drawn = base * np.exp(spread * noise) if base else spread * noise
        out[name] = jnp.asarray(drawn.astype(out[name].dtype))
    for name, factor in factors.items():
        out[name] = (out[name] * factor).astype(out[name].dtype)
    return out
```

```python
from contextlib import ExitStack

import numpy as np

import concourse.bass as bass
from concourse import mybir

F32 = mybir.dt.float32
F16 = mybir.dt.float16
BF16 = mybir.dt.bfloat16
I32 = mybir.dt.int32
ALU = mybir.AluOpType
ACT = mybir.ActivationFunctionType

P = 128
B, T, D, H = 16, 256, 512, 2048
TOK = 512
NB = TOK // T
CHUNKS = B * T // TOK
KT = D // P
SLOTS = H // P
LAG = 2
HBUF = 4
EPS = 1e-5
F16_MAX = 65504.0
RSQRT_MAGIC = float(0x5F3759DF)
NEWTON = 3
LN_STEPS = 2 + 3 * NEWTON
WP = 4
PW = H // WP
STAT_SLOT = [(0, 1), (2, 0), (11, 1), (13, 0)]


def flamingo_block(nc, x_in, v_in, tdf_in, gx_in, gf_in, w1_in, w3_in, w2_in, had_in, out):
    with ExitStack() as ctx:
        def sb(name, shape, dt):
            return ctx.enter_context(nc.sbuf_tensor(name, shape, dt))

        def ps(name, shape):
            return ctx.enter_context(nc.psum_tensor(name, shape, F32))

        def sem(name):
            return ctx.enter_context(nc.semaphore(name))

        w1h, w1l = sb("w1h", [P, WP, KT, PW], F16), sb("w1l", [P, WP, KT, PW], BF16)
        w3h, w3l = sb("w3h", [P, WP, KT, PW], F16), sb("w3l", [P, WP, KT, PW], BF16)
        w2h, w2l = sb("w2h", [P, KT, SLOTS, P], F16), sb("w2l", [P, KT, SLOTS, P], BF16)
        xin = sb("xin", [P, KT, TOK], F32)
        v = sb("v", [P, KT, TOK], F32)
        x1 = sb("x1", [P, 2, KT, TOK], F32)
        xc = sb("xc", [P, KT, TOK], F32)
        ea = sb("ea", [P, KT, TOK], F32)
        eb = sb("eb", [P, KT, TOK], F32)
        bv = sb("bv", [P, KT, TOK], F32)
        psum2 = sb("psum2", [P, 2, TOK], F32)
        ve = sb("ve", [P, TOK], F32)
        rs = sb("rs", [P, TOK], F32)
        nt = sb("nt", [P, TOK], F32)
        xn = sb("xn", [P, 2, KT * TOK], F32)
        xnh = [xn[:, par, 0:KT * TOK // 2].bitcast(F16).rearrange("p (k n) -> p k n", k=KT)
               for par in range(2)]
        xnl = [xn[:, par, KT * TOK // 2:].bitcast(BF16).rearrange("p (k n) -> p k n", k=KT)
               for par in range(2)]
        work = sb("work", [P, 9 * TOK], F32)
        th = work[:, 0:2 * TOK].rearrange("p (b n) -> p b n", b=2)
        hf = work[:, 2 * TOK:4 * TOK].rearrange("p (b n) -> p b n", b=2)
        hh = work[:, 4 * TOK:6 * TOK].bitcast(F16).rearrange("p (b n) -> p b n", b=HBUF)
        hl = work[:, 6 * TOK:8 * TOK].bitcast(BF16).rearrange("p (b n) -> p b n", b=HBUF)
        ug = work[:, 8 * TOK:9 * TOK]
        fwa = work[:, 0:4 * TOK]
        fwb = work[:, 4 * TOK:8 * TOK]
        had = sb("hadamard", [P, 2, P], F32)
        ones = sb("ones", [P, P], F32)
        cc = sb("cc", [P, 6, KT], F32)
        td, tf, exp_td, decay, bias_a, bias_b = (cc[:, i, :] for i in range(6))
        gt = sb("gt", [P, 4], F32)
        raw = [x1[:, 1, :, :].rearrange("p k n -> p (k n)"), xn[:, 1, :]]

        po = ps("po", [P, KT, TOK])
        pg = ps("pg", [P, TOK])
        pl = ps("pl", [P, TOK])
        pst = ps("pst", [P, 2, TOK])

        x_loaded, v_loaded = sem("x_loaded"), sem("v_loaded")
        const_loaded, had_loaded = sem("const_loaded"), sem("had_loaded")
        raw_loaded = [sem("raw_loaded0"), sem("raw_loaded1")]
        out_stored = [sem("out_stored0"), sem("out_stored1")]
        ones_set, biases = sem("ones_set"), sem("biases")
        cst_exp, cst_tanh, cst_decay = sem("cst_exp"), sem("cst_tanh"), sem("cst_decay")
        had_mm = sem("had_mm")
        had_read = sem("had_read")
        fly_add, fly_sub = sem("fly_add"), sem("fly_sub")
        raw_hi, raw_clamped, raw_lo = sem("raw_hi"), sem("raw_clamped"), sem("raw_lo")
        pair_sum, chan_sum = sem("pair_sum"), sem("chan_sum")
        stat = sem("stat")
        centred, squared, normed = sem("centred"), sem("squared"), sem("normed")
        newton = sem("newton")
        exp_a, exp_b = sem("exp_a"), sem("exp_b")
        weighed = sem("weighed")
        scan_b, scan_a = sem("scan_b"), sem("scan_a")
        num_done, den_done = sem("num_done"), sem("den_done")
        rec_done, y_done, x1_done = sem("rec_done"), sem("y_done"), sem("x1_done")
        xn_hi, xn_lo = sem("xn_hi"), sem("xn_lo")
        gate, lin, down = sem("gate"), sem("lin"), sem("down")
        tanhed, gated, hidden = sem("tanhed"), sem("gated"), sem("hidden")
        hid_hi, hid_lo = sem("hid_hi"), sem("hid_lo")
        final = sem("final")

        def wait(eng, s, count):
            if not isinstance(count, int) or count > 0:
                eng.wait_ge(s, count)

        def chunk_loop(eng, body, first=1, last=CHUNKS - 1):
            with eng.Fori(0, (last - first) // 2) as i:
                for k in range(2):
                    body(i * 2 + (first + k), (first + k) % 2, i)

        pieces = [("w2", q) for q in range(KT)] + [(w, p) for p in range(WP) for w in ("w1", "w3")]
        UP0 = KT + 2
        parts = {"w1": (w1h, w1l), "w3": (w3h, w3l), "w2": (w2h, w2l)}

        def hi_of(n):
            return parts[pieces[n][0]][0][:, pieces[n][1], :, :].rearrange("p a b -> p (a b)")

        def lo_of(n):
            return parts[pieces[n][0]][1][:, pieces[n][1], :, :].rearrange("p a b -> p (a b)")

        def split_source(n):
            return fwa if n < KT else raw[n % 2]

        def butterfly_halves(q, stage):
            src, dst = (fwa, fwb) if stage == 0 else (fwb, fwa)
            a = src.rearrange("p (o h i) -> p o h i", h=2, i=TOK // (2 << stage))
            b = dst.rearrange("p (o h i) -> p o h i", h=2, i=TOK // (2 << stage))
            return a[:, :, 0, :], a[:, :, 1, :], b[:, :, 0, :], b[:, :, 1, :]

        block = ctx.enter_context(nc.Block())

        @block.sync
        def _(sp):
            raw_in = {"w1": w1_in, "w3": w3_in, "w2": w2_in}

            def load_weights(n):
                if n >= 2:
                    if n - 2 < KT:
                        sp.wait_ge(had_mm, KT * (n - 1))
                    else:
                        sp.wait_ge(raw_lo, n - 1)
                w, p = pieces[n]
                sp.dma_start(raw[n % 2], raw_in[w][p]).then_inc(raw_loaded[n % 2], 16)

            def load(c):
                sp.wait_ge(x1_done, c * KT)
                sp.dma_start(xin[:, :, :], x_in[c]).then_inc(x_loaded, 16)
                sp.wait_ge(num_done, c * KT)
                sp.dma_start(v[:, :, :], v_in[c]).then_inc(v_loaded, 16)

            def store(c, par):
                sp.wait_ge(final, c * KT + KT)
                sp.dma_start(out[c], x1[:, par, :, :]).then_inc(out_stored[par], 16)

            def steady(c, par, turn):
                store(c - 1, 1 - par)
                load(c + 2)

            sp.dma_start(xin[:, :, :], x_in[0]).then_inc(x_loaded, 16)
            sp.dma_start(cc[:, 0:2, :], tdf_in).then_inc(const_loaded, 16)
            sp.dma_start(gt[:, 0:1], gx_in.partition_broadcast(P)).then_inc(const_loaded, 16)
            sp.dma_start(gt[:, 1:2], gf_in.partition_broadcast(P)).then_inc(const_loaded, 16)
            sp.dma_start(had[:, :, :], had_in).then_inc(had_loaded, 16)
            load_weights(0)
            load_weights(1)
            sp.dma_start(v[:, :, :], v_in[0]).then_inc(v_loaded, 16)
            for n in range(2, UP0 + 2):
                load_weights(n)
            load(1)
            for n in range(UP0 + 2, len(pieces)):
                load_weights(n)
            load(2)
            chunk_loop(sp, steady, last=CHUNKS - 3)
            steady(CHUNKS - 3, 1, None)
            store(CHUNKS - 3 , (CHUNKS - 3) % 2)
            store(CHUNKS - 2, (CHUNKS - 2) % 2)
            store(CHUNKS - 1, (CHUNKS - 1) % 2)
            for par in range(2):
                sp.wait_ge(out_stored[par], 16 * CHUNKS // 2)

        @block.tensor
        def _(pe):
            def statistic(c, k):
                pe.wait_ge(chan_sum, c * 4 + (k + 1))
                if k % 2 == 0:
                    wait(pe, centred, c * 2 + k // 2)
                pe.matmul(pst[:, k % 2, :], ones[:, :], psum2[:, 0, :], start=True,
                          stop=True).then_inc(stat, 1)

            def hadamard(q):
                pe.wait_ge(raw_loaded[q % 2], 16 * (q // 2 + 1))
                for g in range(KT):
                    wait(pe, had_read, KT * (q - 1) + g + 1)
                    for s in range(KT):
                        negated = bin(g & s).count("1") % 2
                        mm = pe.matmul(po[:, g, :], had[:, negated, :],
                                       raw[q % 2][:, s * TOK:(s + 1) * TOK],
                                       start=(s == 0), stop=(s == KT - 1))
                    mm.then_inc(had_mm, 1)

            def up(c, par, j, wh, wl, bank, freed, done):
                wait(pe, freed, c * SLOTS + j)
                piece, col = j // (PW // P), j % (PW // P) * P
                for k in range(KT):
                    hi, lo = wh[:, piece, k, col:col + P], wl[:, piece, k, col:col + P]
                    pe.matmul(bank[:, :], hi, xnh[par][:, k, :], start=(k == 0), stop=False)
                    pe.matmul(bank[:, :], hi, xnl[par][:, k, :], start=False, stop=False)
                    mm = pe.matmul(bank[:, :], lo, xnh[par][:, k, :], start=False,
                                   stop=(k == KT - 1))
                mm.then_inc(done, 1)

            def down_product(c, j):
                pe.wait_ge(hid_hi, c * SLOTS + (j + 1))
                pe.wait_ge(hid_lo, c * SLOTS + (j + 1))
                for d in range(KT):
                    if j == 0:
                        wait(pe, final, c * KT + (d + 1 - KT))
                    b = j % HBUF
                    pe.matmul(po[:, d, :], w2h[:, d, j, :], hh[:, b, :], start=(j == 0), stop=False)
                    pe.matmul(po[:, d, :], w2h[:, d, j, :], hl[:, b, :], start=False, stop=False)
                    mm = pe.matmul(po[:, d, :], w2l[:, d, j, :], hh[:, b, :], start=False,
                                   stop=(j == SLOTS - 1))
                mm.then_inc(down, 1)

            def chunk(c, par, turn, first=False, front=True):
                pe.wait_ge(xn_hi, c + 1)
                pe.wait_ge(xn_lo, c + 1)
                for j in range(SLOTS):
                    if first and j % (PW // P) == 0:
                        pe.wait_ge(raw_clamped, UP0 + 2 * (j * P // PW))
                        pe.wait_ge(raw_lo, UP0 + 2 * (j * P // PW))
                    up(c, par, j, w1h, w1l, pg, gated, gate)
                    for k in range(4):
                        if front and STAT_SLOT[k] == (j, 0):
                            statistic(c + 1, k)
                    up(c, par, j, w3h, w3l, pl, hidden, lin)
                    for k in range(4):
                        if front and STAT_SLOT[k] == (j, 1):
                            statistic(c + 1, k)
                    if j >= LAG:
                        down_product(c, j - LAG)
                    elif not first:
                        down_product(c - 1, SLOTS - LAG + j)

            pe.wait_ge(ones_set, 1)
            statistic(0, 0)
            pe.wait_ge(had_loaded, 16)
            statistic(0, 1)
            for q in range(KT):
                hadamard(q)
            statistic(0, 2)
            statistic(0, 3)
            chunk(0, 0, None, first=True)
            chunk_loop(pe, chunk)
            chunk(CHUNKS - 1, 1, None, front=False)
            for j in range(SLOTS - LAG, SLOTS):
                down_product(CHUNKS - 1, j)

        @block.scalar
        def _(act):
            def squares(c, k):
                act.wait_ge(centred, c * 2 + (k + 1))
                wait(act, chan_sum, c * 4 + 2 * k)
                if k == 1:
                    act.wait_ge(y_done, c * KT + KT)
                act.activation(eb[:, :, :], xc[:, :, :], ACT.Square).then_inc(squared, 1)

            def exps(c, e, bias, done):
                act.wait_ge(normed, c * 2 + 1)
                for k in range(KT):
                    act.activation(e[:, k, :], xc[:, k, :], ACT.Exp,
                                   bias=bias[:, k:k + 1]).then_inc(done, 1)

            def norm_hi(c, par):
                act.wait_ge(normed, c * 2 + 2)
                wait(act, lin, c * SLOTS - SLOTS)
                act.copy(xnh[par], xc[:, :, :]).then_inc(xn_hi, 1)

            def tanh(c, j):
                act.wait_ge(gate, c * SLOTS + (j + 1))
                wait(act, gated, c * SLOTS + (j - 1))
                act.activation(th[:, j % 2, :], pg[:, :], ACT.Tanh, scale=0.5).then_inc(tanhed, 1)

            def weights_hi(n):
                if n < KT:
                    act.wait_ge(fly_add, 2 * n + 2)
                    act.wait_ge(fly_sub, 2 * n + 2)
                else:
                    act.wait_ge(raw_loaded[n % 2], 16 * (n // 2 + 1))
                act.copy(hi_of(n), split_source(n)).then_inc(raw_hi, 1)

            def read_hadamard(q):
                wait(act, raw_lo, q)
                for g in range(KT):
                    act.wait_ge(had_mm, KT * q + g + 1)
                    act.mul(fwa[:, g * TOK:(g + 1) * TOK], po[:, g, :],
                            float(0.5 / np.sqrt(H))).then_inc(had_read, 1)

            def chunk(c, par, turn, first=False, front=True):
                for j in range(SLOTS):
                    tanh(c, j)
                    if first and UP0 + j < len(pieces):
                        weights_hi(UP0 + j)
                    if front:
                        if j == 0:
                            squares(c + 1, 0)
                        elif j == 3:
                            exps(c + 1, ea, bias_a, exp_a)
                            exps(c + 1, eb, bias_b, exp_b)
                        elif j == 11:
                            squares(c + 1, 1)
                        elif j == 14:
                            norm_hi(c + 1, 1 - par)

            act.wait_ge(const_loaded, 48)
            act.activation(exp_td, td, ACT.Exp).then_inc(cst_exp, 1)
            act.activation(gt[:, 2:4], gt[:, 0:2], ACT.Tanh).then_inc(cst_tanh, 1)
            act.wait_ge(cst_exp, 1)
            act.activation(decay, exp_td, ACT.Exp, scale=-1.0).then_inc(cst_decay, 1)
            squares(0, 0)
            act.wait_ge(biases, 2)
            exps(0, ea, bias_a, exp_a)
            exps(0, eb, bias_b, exp_b)
            for q in range(KT):
                read_hadamard(q)
                weights_hi(q)
            weights_hi(KT)
            weights_hi(KT + 1)
            squares(0, 1)
            norm_hi(0, 0)
            chunk(0, 0, None, first=True)
            chunk_loop(act, chunk)
            chunk(CHUNKS - 1, 1, None, front=False)

        @block.vector
        def _(dve):
            def centre(c, k, par):
                dve.wait_ge(stat, c * 4 + (2 * k + 1))
                if k == 0:
                    wait(dve, xn_hi, c)
                    wait(dve, xn_lo, c)
                else:
                    dve.wait_ge(x1_done, c * KT + KT)
                src = xin[:, :, :] if k == 0 else x1[:, par, :, :]
                mean = pst[:, 0:1, :].to_broadcast([P, KT, TOK])
                dve.tensor_tensor(xc[:, :, :], src, mean, ALU.subtract).then_inc(centred, 1)

            def rsqrt(c, k):
                base = c * (2 * LN_STEPS)
                at = k * LN_STEPS
                dve.wait_ge(stat, c * 4 + (2 * k + 2))
                dve.tensor_scalar(ve[:, :], pst[:, 1, :], EPS, None, ALU.add).then_inc(newton, 1)
                dve.wait_ge(newton, base + (at + 1))
                dve.tensor_scalar(rs[:, :].bitcast(I32), ve[:, :].bitcast(I32), -0.5, RSQRT_MAGIC,
                                  ALU.mult, ALU.add).then_inc(newton, 1)
                for s in range(NEWTON):
                    step = at + 2 + 3 * s
                    dve.wait_ge(newton, base + step)
                    dve.tensor_tensor(nt[:, :], rs[:, :], rs[:, :], ALU.mult).then_inc(newton, 1)
                    dve.wait_ge(newton, base + (step + 1))
                    dve.scalar_tensor_tensor(out=nt[:, :], in0=nt[:, :], scalar=-0.5, in1=ve[:, :],
                                             op0=ALU.mult, op1=ALU.mult).then_inc(newton, 1)
                    dve.wait_ge(newton, base + (step + 2))
                    dve.scalar_tensor_tensor(out=rs[:, :], in0=nt[:, :], scalar=1.5, in1=rs[:, :],
                                             op0=ALU.add, op1=ALU.mult).then_inc(newton, 1)

            def normalise(c, k):
                dve.wait_ge(newton, c * (2 * LN_STEPS) + (k + 1) * LN_STEPS)
                dve.wait_ge(squared, c * 2 + (k + 1))
                scale = rs[:, :].unsqueeze(1).to_broadcast([P, KT, TOK])
                dve.tensor_tensor(xc[:, :, :], xc[:, :, :], scale, ALU.mult).then_inc(normed, 1)

            def weigh(c):
                dve.wait_ge(v_loaded, c * 16 + 16)
                dve.wait_ge(exp_b, c * KT + KT)
                dve.tensor_tensor(bv[:, :, :], eb[:, :, :], v[:, :, :], ALU.mult).then_inc(weighed, 1)
                dve.wait_ge(exp_a, c * KT + KT)
                dve.tensor_tensor(v[:, :, :], ea[:, :, :], v[:, :, :], ALU.mult).then_inc(weighed, 1)

            def scan(c, buf, done):
                dve.wait_ge(weighed, c * 2 + 2)
                for k in range(KT):
                    for b in range(NB):
                        seq = buf[:, k, b * T:(b + 1) * T]
                        last = dve.tensor_tensor_scan(seq, decay[:, k:k + 1].to_broadcast([P, T]), seq,
                                                      0.0, ALU.mult, ALU.add)
                    last.then_inc(done, 1)

            def reciprocal(c, k):
                dve.wait_ge(den_done, c * KT + (k + 1))
                dve.reciprocal(eb[:, k, :], eb[:, k, :]).then_inc(rec_done, 1)

            def residual(c, k, par):
                dve.wait_ge(y_done, c * KT + (k + 1))
                dve.scalar_tensor_tensor(out=x1[:, par, k, :], in0=bv[:, k, :], scalar=gt[:, 2:3],
                                         in1=xin[:, k, :], op0=ALU.mult,
                                         op1=ALU.add).then_inc(x1_done, 1)

            def norm_lo(c, par):
                dve.wait_ge(xn_hi, c + 1)
                dve.tensor_tensor(xnl[par], xc[:, :, :], xnh[par], ALU.subtract).then_inc(xn_lo, 1)

            def gate_times(c, j):
                wait(dve, hidden, c * SLOTS + j)
                dve.wait_ge(tanhed, c * SLOTS + (j + 1))
                dve.scalar_tensor_tensor(out=ug, in0=th[:, j % 2, :], scalar=1.0, in1=pg[:, :],
                                         op0=ALU.add, op1=ALU.mult).then_inc(gated, 1)

            def times_lin(c, j):
                dve.wait_ge(lin, c * SLOTS + (j + 1))
                dve.wait_ge(gated, c * SLOTS + (j + 1))
                wait(dve, hid_lo, c * SLOTS + (j - 1))
                dve.tensor_tensor(hf[:, j % 2, :], ug, pl[:, :], ALU.mult).then_inc(hidden, 1)

            def hidden_hi(c, j):
                wait(dve, down, c * SLOTS + (j + 1 - HBUF))
                dve.wait_ge(hidden, c * SLOTS + (j + 1))
                dve.tensor_scalar(hh[:, j % HBUF, :], hf[:, j % 2, :], F16_MAX, -F16_MAX,
                                  ALU.min, ALU.max).then_inc(hid_hi, 1)

            def finish(c, par):
                dve.wait_ge(down, c * SLOTS + SLOTS)
                for d in range(KT):
                    dve.scalar_tensor_tensor(out=x1[:, par, d, :], in0=po[:, d, :], scalar=gt[:, 3:4],
                                             in1=x1[:, par, d, :], op0=ALU.mult,
                                             op1=ALU.add).then_inc(final, 1)

            def clamp(n):
                dve.wait_ge(raw_hi, n + 1)
                dve.tensor_scalar(hi_of(n), hi_of(n), F16_MAX, -F16_MAX, ALU.min,
                                  ALU.max).then_inc(raw_clamped, 1)

            def butterfly_sums(q):
                for stage in range(2):
                    if stage == 0:
                        dve.wait_ge(had_read, KT * q + KT)
                    else:
                        dve.wait_ge(fly_add, 2 * q + 1)
                        dve.wait_ge(fly_sub, 2 * q + 1)
                    a, b, sums, _ = butterfly_halves(q, stage)
                    dve.tensor_tensor(sums, a, b, ALU.add).then_inc(fly_add, 1)

            def chunk(c, par, turn, first=False, front=True):
                for j in range(SLOTS):
                    if j == LAG and not first:
                        finish(c - 1, 1 - par)
                    gate_times(c, j)
                    if j > 0:
                        hidden_hi(c, j - 1)
                    elif not first:
                        hidden_hi(c - 1, SLOTS - 1)
                    if first and UP0 + j < len(pieces):
                        clamp(UP0 + j)
                    if front:
                        if j == 3:
                            normalise(c + 1, 0)
                        if 7 <= j <= 10:
                            reciprocal(c + 1, j - 7)
                        if j == 14:
                            normalise(c + 1, 1)
                    times_lin(c, j)
                    if front:
                        if j == 0:
                            centre(c + 1, 0, 1 - par)
                        elif j == 2:
                            rsqrt(c + 1, 0)
                        elif j == 4:
                            weigh(c + 1)
                        elif j == 5:
                            scan(c + 1, ea, scan_b)
                        elif j == 6:
                            scan(c + 1, v, scan_a)
                            if not first:
                                dve.wait_ge(out_stored[1 - par], turn * 16 + 16)
                        elif 7 <= j <= 10:
                            residual(c + 1, j - 7, 1 - par)
                        elif j == 11:
                            centre(c + 1, 1, 1 - par)
                        elif j == 13:
                            rsqrt(c + 1, 1)
                        elif j == 14:
                            norm_lo(c + 1, 1 - par)

            dve.memset(ones[:, :], 1.0 / D).then_inc(ones_set, 1)
            dve.wait_ge(const_loaded, 48)
            dve.tensor_scalar(bias_a, tf, -1.0, 0.0, ALU.mult, ALU.min).then_inc(biases, 1)
            dve.tensor_scalar(bias_b, tf, 0.0, None, ALU.min).then_inc(biases, 1)
            dve.wait_ge(cst_tanh, 1)
            dve.wait_ge(cst_decay, 1)
            centre(0, 0, 0)
            rsqrt(0, 0)
            normalise(0, 0)
            weigh(0)
            butterfly_sums(0)
            clamp(0)
            scan(0, ea, scan_b)
            butterfly_sums(1)
            clamp(1)
            scan(0, v, scan_a)
            reciprocal(0, 0)
            reciprocal(0, 1)
            butterfly_sums(2)
            clamp(2)
            residual(0, 0, 0)
            reciprocal(0, 2)
            residual(0, 1, 0)
            reciprocal(0, 3)
            residual(0, 2, 0)
            residual(0, 3, 0)
            butterfly_sums(3)
            clamp(3)
            clamp(4)
            clamp(5)
            centre(0, 1, 0)
            rsqrt(0, 1)
            normalise(0, 1)
            norm_lo(0, 0)
            chunk(0, 0, None, first=True)
            chunk_loop(dve, chunk)
            chunk(CHUNKS - 1, 1, CHUNKS // 2 - 1, front=False)
            hidden_hi(CHUNKS - 1, SLOTS - 1)
            finish(CHUNKS - 1, 1)

        @block.gpsimd
        def _(pool):
            def channel_sum(c, k, par):
                if k == 0:
                    pool.wait_ge(x_loaded, c * 16 + 16)
                elif k == 2:
                    pool.wait_ge(x1_done, c * KT + KT)
                else:
                    pool.wait_ge(squared, c * 2 + (k + 1) // 2)
                wait(pool, stat, c * 4 + k)
                src = (xin[:, :, :], eb[:, :, :], x1[:, par, :, :], eb[:, :, :])[k]
                pool.tensor_tensor(psum2[:, :, :], src[:, 0:2, :], src[:, 2:4, :],
                                   ALU.add).then_inc(pair_sum, 1)
                pool.wait_ge(pair_sum, c * 4 + (k + 1))
                pool.tensor_tensor(psum2[:, 0, :], psum2[:, 0, :], psum2[:, 1, :],
                                   ALU.add).then_inc(chan_sum, 1)

            def add_state(c, k, term, state, scanned, done):
                pool.wait_ge(scanned, c * KT + (k + 1))
                t = term[:, k, :].rearrange("p (b t) -> p b t", t=T)
                s = state[:, k, :].rearrange("p (b t) -> p b t", t=T)
                pool.tensor_tensor(t[:, :, 1:T], t[:, :, 1:T], s[:, :, 0:T - 1], ALU.add)
                pool.tensor_tensor(t[:, :, 0:1], t[:, :, 0:1], s[:, :, 0:1],
                                   ALU.add).then_inc(done, 1)

            def quotient(c, k):
                pool.wait_ge(rec_done, c * KT + (k + 1))
                pool.wait_ge(num_done, c * KT + (k + 1))
                pool.tensor_tensor(bv[:, k, :], bv[:, k, :], eb[:, k, :], ALU.mult).then_inc(y_done, 1)

            def hidden_lo(c, j):
                wait(pool, down, c * SLOTS + (j + 1 - HBUF))
                pool.wait_ge(hid_hi, c * SLOTS + (j + 1))
                pool.tensor_tensor(hl[:, j % HBUF, :], hf[:, j % 2, :], hh[:, j % HBUF, :],
                                   ALU.subtract).then_inc(hid_lo, 1)

            def butterfly_differences(q):
                for stage in range(2):
                    if stage == 0:
                        pool.wait_ge(had_read, KT * q + KT)
                    else:
                        pool.wait_ge(fly_add, 2 * q + 1)
                        pool.wait_ge(fly_sub, 2 * q + 1)
                    a, b, _, differences = butterfly_halves(q, stage)
                    pool.tensor_tensor(differences, a, b, ALU.subtract).then_inc(fly_sub, 1)

            def weights_lo(n):
                pool.wait_ge(raw_clamped, n + 1)
                pool.tensor_tensor(lo_of(n), split_source(n), hi_of(n), ALU.subtract).then_inc(raw_lo, 1)

            def chunk(c, par, turn, first=False, front=True):
                for j in range(SLOTS):
                    if front:
                        if j == 0:
                            channel_sum(c + 1, 0, 1 - par)
                        elif j == 1:
                            channel_sum(c + 1, 1, 1 - par)
                        elif j == 6:
                            for k in range(KT):
                                add_state(c + 1, k, eb, ea, scan_b, den_done)
                        elif j == 7:
                            for k in range(KT):
                                add_state(c + 1, k, bv, v, scan_a, num_done)
                            quotient(c + 1, 0)
                        elif 8 <= j <= 10:
                            quotient(c + 1, j - 7)
                        elif j == 11:
                            channel_sum(c + 1, 2, 1 - par)
                        elif j == 12:
                            channel_sum(c + 1, 3, 1 - par)
                    if first and UP0 + j < len(pieces):
                        weights_lo(UP0 + j)
                    hidden_lo(c, j)

            channel_sum(0, 0, 0)
            channel_sum(0, 1, 0)
            butterfly_differences(0)
            weights_lo(0)
            for k in range(KT):
                add_state(0, k, eb, ea, scan_b, den_done)
            butterfly_differences(1)
            weights_lo(1)
            for k in range(KT):
                add_state(0, k, bv, v, scan_a, num_done)
            quotient(0, 0)
            butterfly_differences(2)
            weights_lo(2)
            for k in range(1, KT):
                quotient(0, k)
            butterfly_differences(3)
            weights_lo(3)
            weights_lo(4)
            weights_lo(5)
            channel_sum(0, 2, 0)
            channel_sum(0, 3, 0)
            chunk(0, 0, None, first=True)
            chunk_loop(pool, chunk)
            chunk(CHUNKS - 1, 1, None, front=False)


def kernel(x, ctx_2048, g_xattn, g_ffn, L0_xattn_time_decay, L0_xattn_time_first,
           L0_ffn_W1, L0_ffn_W2, L0_ffn_W3):
    import concourse.bacc as bacc
    from concourse.bass_utils import run_bass_kernel_spmd

    def chunked(a):
        return np.ascontiguousarray(
            np.asarray(a).reshape(CHUNKS, TOK, KT, P).transpose(0, 3, 2, 1))

    def up_layout(w):
        return np.ascontiguousarray(
            np.asarray(w).reshape(WP, PW, KT, P).transpose(0, 3, 2, 1).reshape(WP, P, KT * PW))

    w2 = np.asarray(L0_ffn_W2).reshape(KT, P, SLOTS, P).transpose(0, 3, 2, 1).reshape(KT, P, SLOTS * P)
    per_channel = np.stack([np.asarray(L0_xattn_time_decay).reshape(KT, P).T,
                            np.asarray(L0_xattn_time_first).reshape(KT, P).T], axis=1)
    had = np.ones((1, 1), np.float32)
    while had.shape[0] < P:
        had = np.block([[had, had], [had, -had]])
    arrays = {
        "x_t": chunked(x), "ctx_t": chunked(ctx_2048), "tdf": np.ascontiguousarray(per_channel),
        "gx": np.asarray(g_xattn), "gf": np.asarray(g_ffn),
        "w1_t": up_layout(L0_ffn_W1), "w3_t": up_layout(L0_ffn_W3), "w2_t": np.ascontiguousarray(w2),
        "had_in": np.ascontiguousarray(np.stack([had, -had], axis=1)),
    }
    nc = bacc.Bacc("TRN2", target_bir_lowering=False, num_devices=1)
    args = [nc.dram_tensor(name, a.shape, F32, kind="ExternalInput").ap() for name, a in arrays.items()]
    out = nc.dram_tensor("out_t", (CHUNKS, P, KT, TOK), F32, kind="ExternalOutput").ap()
    flamingo_block(nc, *args, out)
    got = run_bass_kernel_spmd(nc, [arrays], core_ids=[0]).results[0]["out_t"]
    return np.asarray(got).transpose(0, 3, 2, 1).reshape(B, T, D)
```

```python
from contextlib import ExitStack

import numpy as np

import concourse.bass as bass
from concourse import mybir

F32 = mybir.dt.float32
F16 = mybir.dt.float16
BF16 = mybir.dt.bfloat16
I32 = mybir.dt.int32
ALU = mybir.AluOpType
ACT = mybir.ActivationFunctionType

P = 128
B, T, D, H = 16, 256, 512, 2048
TOK = 512
NB = TOK // T
CHUNKS = B * T // TOK
RUNS = CHUNKS + 1
KT = D // P
SLOTS = H // P
LAG = 2
HBUF = 4
EPS = 1e-5
F16_MAX = 65504.0
RSQRT_MAGIC = float(0x5F3759DF)
NEWTON = 3
NEWTON_FIRST = 2
LN_STEPS = 2 + 3 * NEWTON
WP = 4
PW = H // WP
FLYS = (3, 2, 2, 3)
STAT_STEP = [(0, 1), (2, 0), (11, 1), (13, 0)]
FRONT1_AT = (0, 0, 1, 2, 4, 4, 5, 6, 6, 7, 8, 9, 9, 10, 11, 11)
FRONT2_AT = (12, 13, 15, 16, 18, 19, 20, 22, 23, 24, 25, 27, 28, 29, 30, 31)
SPLIT_SLOT = {1: 6, 2: 7, 3: 8, 5: 9, 6: 10, 8: 11}
LO_ON_VECTOR = (4, 5, 7, 9, 11)


def flamingo_block(nc, x_in, v_in, tdf_in, gx_in, gf_in, w1_in, w3_in, w2_in, had_in, out):
    with ExitStack() as ctx:
        def sb(name, shape, dt):
            return ctx.enter_context(nc.sbuf_tensor(name, shape, dt))

        def ps(name, shape):
            return ctx.enter_context(nc.psum_tensor(name, shape, F32))

        def sem(name):
            return ctx.enter_context(nc.semaphore(name))

        w1h, w1l = sb("w1h", [P, WP, KT, PW], F16), sb("w1l", [P, WP, KT, PW], BF16)
        w3h, w3l = sb("w3h", [P, WP, KT, PW], F16), sb("w3l", [P, WP, KT, PW], BF16)
        w2h, w2l = sb("w2h", [P, KT, SLOTS, P], F16), sb("w2l", [P, KT, SLOTS, P], BF16)
        xin = sb("xin", [P, KT, TOK], F32)
        v = sb("v", [P, KT, TOK], F32)
        x1 = sb("x1", [P, 2, KT, TOK], F32)
        xc = sb("xc", [P, KT, TOK], F32)
        ea = sb("ea", [P, KT, TOK], F32)
        eb = sb("eb", [P, KT, TOK], F32)
        bv = sb("bv", [P, KT, TOK], F32)
        psum2 = sb("psum2", [P, 2, TOK], F32)
        var_eps = sb("var_eps", [P, TOK], F32)
        rstd = sb("rstd", [P, TOK], F32)
        newton_tmp = sb("newton_tmp", [P, TOK], F32)
        xn = sb("xn", [P, 2, KT * TOK], F32)
        xnh = [xn[:, par, 0:KT * TOK // 2].bitcast(F16).rearrange("p (k n) -> p k n", k=KT)
               for par in range(2)]
        xnl = [xn[:, par, KT * TOK // 2:].bitcast(BF16).rearrange("p (k n) -> p k n", k=KT)
               for par in range(2)]
        work = sb("work", [P, 9 * TOK], F32)
        th = work[:, 0:2 * TOK].rearrange("p (b n) -> p b n", b=2)
        hf = work[:, 2 * TOK:4 * TOK].rearrange("p (b n) -> p b n", b=2)
        hh = work[:, 4 * TOK:6 * TOK].bitcast(F16).rearrange("p (b n) -> p b n", b=HBUF)
        hl = work[:, 6 * TOK:8 * TOK].bitcast(BF16).rearrange("p (b n) -> p b n", b=HBUF)
        ug = work[:, 8 * TOK:9 * TOK]
        had = sb("hadamard", [P, 2, P], F32)
        ones = sb("ones", [P, P], F32)
        cc = sb("cc", [P, 6, KT], F32)
        td, tf, exp_td, decay, bias_a, bias_b = (cc[:, i, :] for i in range(6))
        gt = sb("gt", [P, 4], F32)
        def last_pieces(w):
            return w[:, WP // 2:, :, :].rearrange("p a k n -> p (a k n)").bitcast(F32)

        raw = [x1[:, 1, :, :].rearrange("p k n -> p (k n)"), xn[:, 1, :],
               work[:, 0:4 * TOK], work[:, 4 * TOK:8 * TOK]]
        fw = [(last_pieces(w3h), last_pieces(w3l)), (last_pieces(w1h), last_pieces(w1l))]

        po = ps("po", [P, KT, TOK])
        pg = ps("pg", [P, TOK])
        pl = ps("pl", [P, TOK])
        pst = ps("pst", [P, 2, TOK])

        x_half, v_half = ([sem(f"{name}_half{h}") for h in range(2)] for name in "xv")
        x_loaded, v_loaded = sem("x_loaded"), sem("v_loaded")
        const_loaded, had_loaded = sem("const_loaded"), sem("had_loaded")
        raw_loaded = [sem(f"raw_loaded{i}") for i in range(4)]
        out_stored = [sem("out_stored0"), sem("out_stored1")]
        ones_set, biases = sem("ones_set"), sem("biases")
        cst_exp, cst_tanh, cst_decay = sem("cst_exp"), sem("cst_tanh"), sem("cst_decay")
        had_mm = sem("had_mm")
        had_read = sem("had_read")
        fly_add, fly_sub = sem("fly_add"), sem("fly_sub")
        raw_hi, raw_clamped = sem("raw_hi"), sem("raw_clamped")
        raw_lo_vector, raw_lo_pool = sem("raw_lo_vector"), sem("raw_lo_pool")
        pair_sum, chan_sum = sem("pair_sum"), sem("chan_sum")
        stat = sem("stat")
        centred, squared, normed = sem("centred"), sem("squared"), sem("normed")
        newton = sem("newton")
        exp_a, exp_b = sem("exp_a"), sem("exp_b")
        weighed = sem("weighed")
        scan_b, scan_a = sem("scan_b"), sem("scan_a")
        num_done, den_done = sem("num_done"), sem("den_done")
        rec_done, y_done, x1_done = sem("rec_done"), sem("y_done"), sem("x1_done")
        xn_hi, xn_lo = sem("xn_hi"), sem("xn_lo")
        gate, lin, down = sem("gate"), sem("lin"), sem("down")
        tanhed, gated, hidden = sem("tanhed"), sem("gated"), sem("hidden")
        hid_hi, hid_lo = sem("hid_hi"), sem("hid_lo")
        final = sem("final")
        down_tail, tail_stored = sem("down_tail"), sem("tail_stored")

        def wait(eng, s, count):
            if not isinstance(count, int) or count > 0:
                eng.wait_ge(s, count)

        class Run:
            def __init__(self, r, par=0, turn=0):
                self.r, self.par, self.turn = r, par, turn
                self.half = isinstance(r, int) and r < 2
                self.cols = slice(r * T, r * T + T) if self.half else slice(0, TOK)
                self.n = T if self.half else TOK
                self.batches = (r,) if self.half else range(NB)

            def previous(self):
                return Run(0) if self.half else Run(self.r - 1, 1 - self.par)

            def tile(self, j):
                return self.r * SLOTS + (j + 1)

            def downs(self, j):
                if self.half and self.r == 0:
                    return j + 1
                return self.r * SLOTS + (j + 1 - LAG)

            def nth(self, k, of):
                return self.r * of + (k + 1)

        def run_loop(eng, body, last=RUNS - 1):
            with eng.Fori(0, (last - 2) // 2) as i:
                for k in range(2):
                    body(Run(i * 2 + (2 + k), 1 - k, i))

        def front_steps(run, j):
            if not run.half:
                ahead = Run(run.r + 1, 1 - run.par, run.turn)
                return [(ahead, j)]
            at = run.r * SLOTS + j
            return ([(Run(1), step) for step in range(SLOTS) if FRONT1_AT[step] == at] +
                    [(Run(2, 1), step) for step in range(SLOTS) if FRONT2_AT[step] == at])

        pieces = [("w1", 0), ("w3", 0)] + [("w2", q) for q in range(KT)]
        pieces += [(w, p) for p in range(1, WP) for w in ("w1", "w3")]
        W2_0, LATE = 2, 2 + KT
        place = [2, 3] + [0, 1] * (len(pieces) // 2 - 1)
        loads = [place[:n + 1].count(place[n]) for n in range(len(pieces))]
        parts = {"w1": (w1h, w1l), "w3": (w3h, w3l), "w2": (w2h, w2l)}

        def wait_split(eng, n):
            on_vector = sum(m < n for m in LO_ON_VECTOR)
            wait(eng, raw_lo_vector, on_vector)
            wait(eng, raw_lo_pool, n - on_vector)

        def hi_of(n):
            return parts[pieces[n][0]][0][:, pieces[n][1], :, :].rearrange("p a b -> p (a b)")

        def lo_of(n):
            return parts[pieces[n][0]][1][:, pieces[n][1], :, :].rearrange("p a b -> p (a b)")

        def split_source(n):
            q = n - W2_0
            return fw[q % 2][FLYS[q] % 2] if pieces[n][0] == "w2" else raw[place[n]]

        def weights_lo(eng, n, done):
            eng.wait_ge(raw_clamped, n + 1)
            eng.tensor_tensor(lo_of(n), split_source(n), hi_of(n), ALU.subtract).then_inc(done, 1)

        def butterfly(eng, q, stage, op, half, done):
            if stage == 0:
                eng.wait_ge(had_read, KT * q + KT)
                if q >= 2:
                    wait_split(eng, W2_0 + q - 1)
            else:
                eng.wait_ge(fly_add, sum(FLYS[:q]) + stage)
                eng.wait_ge(fly_sub, sum(FLYS[:q]) + stage)
            src, dst = (fw[q % 2][(stage + i) % 2] for i in range(2))
            inner = P << (FLYS[q] - 1 - stage)
            a = src.rearrange("p (o h i) -> p o h i", h=2, i=inner)
            b = dst.rearrange("p (o h i) -> p o h i", h=2, i=inner)
            eng.tensor_tensor(b[:, :, half, :], a[:, :, 0, :], a[:, :, 1, :], op).then_inc(done, 1)

        last_stages = (range(2), range(2, FLYS[-1]))

        block = ctx.enter_context(nc.Block())

        @block.sync
        def _(sp):
            raw_in = {"w1": w1_in, "w3": w3_in, "w2": w2_in}

            def load_weights(n):
                if W2_0 + 2 <= n < LATE + 2:
                    sp.wait_ge(had_mm, KT * (n - W2_0 - 1))
                elif n >= LATE + 2:
                    wait_split(sp, n - 1)
                w, p = pieces[n]
                sp.dma_start(raw[place[n]], raw_in[w][p]).then_inc(raw_loaded[place[n]], 16)

            def load_half(dst, src, half, loaded):
                cols = slice(half * T, half * T + T)
                sp.dma_start(dst[:, :, cols], src[0][:, :, cols]).then_inc(loaded[half], 16)

            def load(c):
                sp.wait_ge(x1_done, c * KT + KT)
                sp.dma_start(xin[:, :, :], x_in[c]).then_inc(x_loaded, 16)
                sp.wait_ge(num_done, c * KT + KT)
                sp.dma_start(v[:, :, :], v_in[c]).then_inc(v_loaded, 16)

            def store(c, par):
                sp.wait_ge(final, c * KT + KT)
                sp.dma_start(out[c], x1[:, par, :, :]).then_inc(out_stored[par], 16)

            def steady(run):
                store(run.r - 2, 1 - run.par)
                load(run.r + 1)

            load_half(xin, x_in, 0, x_half)
            load_weights(0)
            sp.dma_start(cc[:, 0:2, :], tdf_in).then_inc(const_loaded, 16)
            sp.dma_start(gt[:, 0:1], gx_in.partition_broadcast(P)).then_inc(const_loaded, 16)
            sp.dma_start(gt[:, 1:2], gf_in.partition_broadcast(P)).then_inc(const_loaded, 16)
            sp.dma_start(had[:, :, :], had_in).then_inc(had_loaded, 16)
            load_weights(W2_0)
            load_weights(1)
            load_half(v, v_in, 0, v_half)
            load_weights(W2_0 + 1)
            load_half(xin, x_in, 1, x_half)
            load_half(v, v_in, 1, v_half)
            for n in range(W2_0 + 2, LATE):
                load_weights(n)
            for n in range(LATE, len(pieces)):
                load_weights(n)
            load(1)
            load(2)
            run_loop(sp, steady, last=RUNS - 3)
            steady(Run(RUNS - 3, 1))
            store(CHUNKS - 3, 1)
            store(CHUNKS - 2, 0)
            for d in range(KT):
                sp.wait_ge(final, CHUNKS * KT - KT + d + 1)
                sp.dma_start(out[CHUNKS - 1][:, d, :], x1[:, 1, d, :]).then_inc(tail_stored, 16)
            sp.wait_ge(out_stored[0], 16 * (CHUNKS // 2))
            sp.wait_ge(out_stored[1], 16 * (CHUNKS // 2 - 1))
            sp.wait_ge(tail_stored, 16 * KT)

        @block.tensor
        def _(pe):
            def statistic(run, k):
                bank = pst[:, k % 2, run.cols]
                if run.half:
                    if k == 0:
                        pe.wait_ge(x_half[run.r], 16)
                    elif k == 2:
                        pe.wait_ge(x1_done, run.nth(KT - 1, KT))
                    else:
                        pe.wait_ge(squared, run.nth(k // 2, 2))
                    src = (xin, eb, x1[:, 0, :, :], eb)[k][:, :, run.cols]
                    for t in range(KT):
                        mm = pe.matmul(bank, ones[:, :], src[:, t, :], start=(t == 0),
                                       stop=(t == KT - 1))
                    mm.then_inc(stat, 1)
                else:
                    pe.wait_ge(chan_sum, run.nth(k, 4) - 8)
                    if k % 2 == 0:
                        pe.wait_ge(centred, run.nth(k // 2, 2) - 1)
                    pe.matmul(bank, ones[:, :], psum2[:, 0, :], start=True, stop=True).then_inc(stat, 1)

            def hadamard(q, g):
                bits = KT - 1 if FLYS[q] == 2 else KT // 2
                n = W2_0 + q
                pe.wait_ge(raw_loaded[place[n]], 16 * loads[n])
                wait(pe, had_read, KT * (q - 1) + g + 1)
                sources = [s for s in range(KT) if (s ^ g) & ~bits == 0]
                for s in sources:
                    negated = bin(g & s & bits).count("1") % 2
                    mm = pe.matmul(po[:, g, :], had[:, negated, :],
                                   raw[place[n]][:, s * TOK:(s + 1) * TOK],
                                   start=(s == sources[0]), stop=(s == sources[-1]))
                mm.then_inc(had_mm, 1)

            def up(run, j, wh, wl, bank, freed, done):
                wait(pe, freed, run.tile(j - 1))
                piece, col = j // (PW // P), j % (PW // P) * P
                for k in range(KT):
                    hi, lo = wh[:, piece, k, col:col + P], wl[:, piece, k, col:col + P]
                    nh, nl = xnh[run.par][:, k, run.cols], xnl[run.par][:, k, run.cols]
                    pe.matmul(bank[:, 0:run.n], hi, nh, start=(k == 0), stop=False)
                    pe.matmul(bank[:, 0:run.n], hi, nl, start=False, stop=False)
                    mm = pe.matmul(bank[:, 0:run.n], lo, nh, start=False, stop=(k == KT - 1))
                mm.then_inc(done, 1)

            def down_tile(run, j, d):
                b, first = j % HBUF, j == 0 and not (run.half and run.r == 1)
                acc, h, l = po[:, d, run.cols], hh[:, b, run.cols], hl[:, b, run.cols]
                pe.matmul(acc, w2h[:, d, j, :], h, start=first, stop=False, skip_group_check=True)
                pe.matmul(acc, w2h[:, d, j, :], l, start=False, stop=False, skip_group_check=True)
                return pe.matmul(acc, w2l[:, d, j, :], h, start=False, stop=(j == SLOTS - 1),
                                 skip_group_check=True)

            def down_product(run, j):
                pe.wait_ge(hid_hi, run.tile(j))
                pe.wait_ge(hid_lo, run.tile(j))
                for d in range(KT):
                    if j == 0 and not run.half:
                        pe.wait_ge(final, run.nth(d, KT) - 2 * KT)
                    mm = down_tile(run, j, d)
                mm.then_inc(down, 1)

            def statistics(steps, place):
                for ahead, step in steps:
                    if (step, place) in STAT_STEP:
                        statistic(ahead, STAT_STEP.index((step, place)))

            def ffn(run, front=True):
                pe.wait_ge(xn_hi, run.nth(0, 1))
                pe.wait_ge(xn_lo, run.nth(0, 1))
                for j in range(SLOTS):
                    steps = front_steps(run, j) if front else []
                    if run.half and run.r == 0:
                        if j % (PW // P) == 0:
                            wait_split(pe, LATE + 2 * (j * P // PW) if j else W2_0)
                        if j == LAG:
                            wait_split(pe, LATE)
                    up(run, j, w1h, w1l, pg, gated, gate)
                    if not run.half:
                        statistics(steps, 0)
                    up(run, j, w3h, w3l, pl, hidden, lin)
                    if not run.half:
                        statistics(steps, 1)
                    if j >= LAG:
                        down_product(run, j - LAG)
                    elif not run.half:
                        down_product(run.previous(), SLOTS - LAG + j)
                    if run.half:
                        statistics(steps, 0)
                        statistics(steps, 1)

            pe.wait_ge(ones_set, 1)
            statistic(Run(0), 0)
            statistic(Run(0), 1)
            pe.wait_ge(had_loaded, 16)
            for q in range(2):
                for g in range(KT):
                    hadamard(q, g)
            hadamard(2, 0)
            statistic(Run(0), 2)
            hadamard(2, 1)
            statistic(Run(0), 3)
            hadamard(2, 2)
            hadamard(2, 3)
            for g in range(KT):
                hadamard(3, g)
            ffn(Run(0))
            ffn(Run(1))
            run_loop(pe, ffn)
            last = Run(RUNS - 1, 1)
            ffn(last, front=False)
            for d in range(KT):
                for j in range(SLOTS - LAG, SLOTS):
                    pe.wait_ge(hid_hi, last.tile(j))
                    pe.wait_ge(hid_lo, last.tile(j))
                    mm = down_tile(last, j, d)
                mm.then_inc(down_tail, 1)

        @block.scalar
        def _(act):
            def squares(run, k):
                act.wait_ge(centred, run.nth(k, 2))
                act.activation(eb[:, :, run.cols], xc[:, :, run.cols], ACT.Square).then_inc(squared, 1)

            def exps(run, e, bias, done):
                act.wait_ge(normed, run.nth(0, 2))
                for k in range(KT):
                    act.activation(e[:, k, run.cols], xc[:, k, run.cols], ACT.Exp,
                                   bias=bias[:, k:k + 1]).then_inc(done, 1)

            def norm_hi(run):
                act.wait_ge(normed, run.nth(1, 2))
                if not run.half:
                    act.wait_ge(lin, run.tile(-1) - SLOTS)
                act.copy(xnh[run.par][:, :, run.cols], xc[:, :, run.cols]).then_inc(xn_hi, 1)

            def tanh(run, j):
                act.wait_ge(gate, run.tile(j))
                wait(act, gated, run.tile(j - 2))
                act.activation(th[:, j % 2, 0:run.n], pg[:, 0:run.n], ACT.Tanh,
                               scale=0.5).then_inc(tanhed, 1)

            def weights_hi(n):
                if pieces[n][0] == "w2":
                    flown = sum(FLYS[:n - W2_0 + 1])
                    act.wait_ge(fly_add, flown)
                    act.wait_ge(fly_sub, flown)
                else:
                    act.wait_ge(raw_loaded[place[n]], 16 * loads[n])
                if n == LATE + 2:
                    wait_split(act, LATE)
                act.copy(hi_of(n), split_source(n)).then_inc(raw_hi, 1)

            def read_hadamard(q):
                if q >= 2:
                    act.wait_ge(fly_add, sum(FLYS[:q - 1]))
                    act.wait_ge(fly_sub, sum(FLYS[:q - 1]))
                    if FLYS[q - 2] % 2 == 0:
                        wait_split(act, W2_0 + q - 1)
                for g in range(KT):
                    act.wait_ge(had_mm, KT * q + g + 1)
                    act.mul(fw[q % 2][0][:, g * TOK:(g + 1) * TOK], po[:, g, :],
                            float(0.5 / np.sqrt(H))).then_inc(had_read, 1)

            def front_step(run, step):
                if step == 0:
                    squares(run, 0)
                elif step == 11:
                    squares(run, 1)
                elif step == 14:
                    norm_hi(run)

            def ffn(run, front=True):
                for j in range(SLOTS):
                    tanh(run, j)
                    for ahead, step in front_steps(run, j) if front else []:
                        front_step(ahead, step)
                        if step == 3 and not run.half:
                            exps(ahead, eb, bias_b, exp_b)
                            exps(ahead, ea, bias_a, exp_a)
                        elif step == 4 and run.half:
                            exps(ahead, ea, bias_a, exp_a)
                    if run.half and j > 0:
                        for ahead, step in front_steps(run, j - 1):
                            if step == 3:
                                exps(ahead, eb, bias_b, exp_b)
                    if run.half and run.r == 0:
                        if j == 1:
                            weights_hi(LATE - 1)
                        if j in SPLIT_SLOT:
                            weights_hi(SPLIT_SLOT[j])

            act.wait_ge(const_loaded, 48)
            act.activation(exp_td, td, ACT.Exp).then_inc(cst_exp, 1)
            act.activation(gt[:, 2:4], gt[:, 0:2], ACT.Tanh).then_inc(cst_tanh, 1)
            act.wait_ge(cst_exp, 1)
            act.activation(decay, exp_td, ACT.Exp, scale=-1.0).then_inc(cst_decay, 1)
            act.wait_ge(biases, 2)
            weights_hi(0)
            squares(Run(0), 0)
            weights_hi(1)
            read_hadamard(0)
            exps(Run(0), eb, bias_b, exp_b)
            exps(Run(0), ea, bias_a, exp_a)
            read_hadamard(1)
            squares(Run(0), 1)
            weights_hi(2)
            weights_hi(3)
            read_hadamard(2)
            norm_hi(Run(0))
            weights_hi(4)
            read_hadamard(3)
            ffn(Run(0))
            ffn(Run(1))
            run_loop(act, ffn)
            ffn(Run(RUNS - 1, 1), front=False)

        @block.vector
        def _(dve):
            def centre(run, k):
                dve.wait_ge(stat, run.nth(2 * k, 4))
                if k == 0:
                    wait(dve, xn_hi, run.r)
                    wait(dve, xn_lo, run.r)
                else:
                    dve.wait_ge(x1_done, run.nth(KT - 1, KT))
                src = (xin if k == 0 else x1[:, run.par, :, :])[:, :, run.cols]
                mean = pst[:, 0:1, run.cols].to_broadcast([P, KT, run.n])
                dve.tensor_tensor(xc[:, :, run.cols], src, mean, ALU.subtract).then_inc(centred, 1)

            def rsqrt(run, k, steps):
                base = run.r * (2 * LN_STEPS)
                at = k * LN_STEPS
                ve, rs, nt = (buf[:, 0:run.n] for buf in (var_eps, rstd, newton_tmp))
                if 0 in steps:
                    dve.wait_ge(stat, run.nth(2 * k + 1, 4))
                    dve.tensor_scalar(ve, pst[:, 1, run.cols], EPS, None, ALU.add).then_inc(newton, 1)
                    dve.wait_ge(newton, base + (at + 1))
                    dve.tensor_scalar(rs.bitcast(I32), ve.bitcast(I32), -0.5, RSQRT_MAGIC,
                                      ALU.mult, ALU.add).then_inc(newton, 1)
                for s in steps:
                    step = at + 2 + 3 * s
                    dve.wait_ge(newton, base + step)
                    dve.tensor_tensor(nt, rs, rs, ALU.mult).then_inc(newton, 1)
                    dve.wait_ge(newton, base + (step + 1))
                    dve.scalar_tensor_tensor(out=nt, in0=nt, scalar=-0.5, in1=ve,
                                             op0=ALU.mult, op1=ALU.mult).then_inc(newton, 1)
                    dve.wait_ge(newton, base + (step + 2))
                    dve.scalar_tensor_tensor(out=rs, in0=nt, scalar=1.5, in1=rs,
                                             op0=ALU.add, op1=ALU.mult).then_inc(newton, 1)

            def normalise(run, k):
                dve.wait_ge(newton, run.nth(k, 2) * LN_STEPS)
                dve.wait_ge(squared, run.nth(k, 2))
                scale = rstd[:, 0:run.n].unsqueeze(1).to_broadcast([P, KT, run.n])
                dve.tensor_tensor(xc[:, :, run.cols], xc[:, :, run.cols], scale,
                                  ALU.mult).then_inc(normed, 1)

            def weigh(run):
                if run.half:
                    dve.wait_ge(v_half[run.r], 16)
                else:
                    dve.wait_ge(v_loaded, run.r * 16 - 16)
                cols = run.cols
                dve.wait_ge(exp_b, run.nth(KT - 1, KT))
                dve.tensor_tensor(bv[:, :, cols], eb[:, :, cols], v[:, :, cols],
                                  ALU.mult).then_inc(weighed, 1)
                dve.wait_ge(exp_a, run.nth(KT - 1, KT))
                dve.tensor_tensor(v[:, :, cols], ea[:, :, cols], v[:, :, cols],
                                  ALU.mult).then_inc(weighed, 1)

            def scan(run, buf, done):
                dve.wait_ge(weighed, run.nth(1, 2))
                for k in range(KT):
                    for b in run.batches:
                        seq = buf[:, k, b * T:(b + 1) * T]
                        last = dve.tensor_tensor_scan(seq, decay[:, k:k + 1].to_broadcast([P, T]), seq,
                                                      0.0, ALU.mult, ALU.add)
                    last.then_inc(done, 1)

            def reciprocal(run, k):
                dve.wait_ge(den_done, run.nth(k, KT))
                dve.reciprocal(eb[:, k, run.cols], eb[:, k, run.cols]).then_inc(rec_done, 1)

            def residual(run, k):
                dve.wait_ge(y_done, run.nth(k, KT))
                if k == 0 and not run.half:
                    wait_split(dve, len(pieces))
                dve.scalar_tensor_tensor(out=x1[:, run.par, k, run.cols], in0=bv[:, k, run.cols],
                                         scalar=gt[:, 2:3], in1=xin[:, k, run.cols], op0=ALU.mult,
                                         op1=ALU.add).then_inc(x1_done, 1)

            def norm_lo(run):
                dve.wait_ge(xn_hi, run.nth(0, 1))
                dve.tensor_tensor(xnl[run.par][:, :, run.cols], xc[:, :, run.cols],
                                  xnh[run.par][:, :, run.cols], ALU.subtract).then_inc(xn_lo, 1)

            def gate_times(run, j):
                wait(dve, hidden, run.tile(j - 1))
                dve.wait_ge(tanhed, run.tile(j))
                dve.scalar_tensor_tensor(out=ug[:, 0:run.n], in0=th[:, j % 2, 0:run.n], scalar=1.0,
                                         in1=pg[:, 0:run.n], op0=ALU.add,
                                         op1=ALU.mult).then_inc(gated, 1)

            def times_lin(run, j):
                dve.wait_ge(lin, run.tile(j))
                dve.wait_ge(gated, run.tile(j))
                wait(dve, hid_lo, run.tile(j - 2))
                dve.tensor_tensor(hf[:, j % 2, run.cols], ug[:, 0:run.n], pl[:, 0:run.n],
                                  ALU.mult).then_inc(hidden, 1)

            def hidden_hi(run, j):
                if not run.half or j >= HBUF:
                    dve.wait_ge(down, run.downs(j - HBUF))
                dve.wait_ge(hidden, run.tile(j))
                dve.tensor_scalar(hh[:, j % HBUF, run.cols], hf[:, j % 2, run.cols], F16_MAX, -F16_MAX,
                                  ALU.min, ALU.max).then_inc(hid_hi, 1)

            def finish(c, par, d, done, count):
                dve.wait_ge(done, count)
                dve.scalar_tensor_tensor(out=x1[:, par, d, :], in0=po[:, d, :], scalar=gt[:, 3:4],
                                         in1=x1[:, par, d, :], op0=ALU.mult,
                                         op1=ALU.add).then_inc(final, 1)

            def clamp(n):
                dve.wait_ge(raw_hi, n + 1)
                dve.tensor_scalar(hi_of(n), hi_of(n), F16_MAX, -F16_MAX, ALU.min,
                                  ALU.max).then_inc(raw_clamped, 1)

            def sums(q, stage):
                butterfly(dve, q, stage, ALU.add, 0, fly_add)

            def front_step(run, step, early, late, first_newton):
                if early:
                    if step == 3:
                        rsqrt(run, 0, range(first_newton, NEWTON))
                        normalise(run, 0)
                    elif 7 <= step <= 10:
                        reciprocal(run, step - 7)
                    elif step == 14:
                        rsqrt(run, 1, range(first_newton, NEWTON))
                        normalise(run, 1)
                if late:
                    if step == 0:
                        centre(run, 0)
                    elif step == 2:
                        rsqrt(run, 0, range(first_newton))
                    elif step == 4:
                        weigh(run)
                    elif step == 5:
                        scan(run, ea, scan_b)
                    elif step == 6:
                        scan(run, v, scan_a)
                        if not isinstance(run.r, int):
                            dve.wait_ge(out_stored[run.par], run.turn * 16 + 16)
                    elif 9 <= step <= 10:
                        residual(run, 2 * step - 18)
                        residual(run, 2 * step - 17)
                    elif step == 11:
                        centre(run, 1)
                    elif step == 13:
                        rsqrt(run, 1, range(first_newton))
                    elif step == 14:
                        norm_lo(run)

            def ffn(run, front=True):
                for j in range(SLOTS):
                    steps = front_steps(run, j) if front else []
                    if j == LAG and not run.half:
                        for d in range(KT):
                            finish(run.r - 2, 1 - run.par, d, down, run.downs(-1))
                    gate_times(run, j)
                    if j > 0:
                        hidden_hi(run, j - 1)
                    elif not run.half or run.r > 0:
                        hidden_hi(run.previous(), SLOTS - 1)
                    if not run.half:
                        for ahead, step in steps:
                            front_step(ahead, step, True, False, NEWTON)
                    times_lin(run, j)
                    for ahead, step in steps:
                        if run.half:
                            front_step(ahead, step, True, True, NEWTON_FIRST)
                        else:
                            front_step(ahead, step, False, True, NEWTON)
                    if run.half and run.r == 0 and j < 2:
                        for stage in last_stages[j]:
                            sums(KT - 1, stage)
                        if j == 1:
                            clamp(LATE - 1)
                            weights_lo(dve, LATE - 1, raw_lo_vector)
                    if run.half and run.r == 0 and j in SPLIT_SLOT:
                        clamp(SPLIT_SLOT[j])
                        if SPLIT_SLOT[j] in LO_ON_VECTOR:
                            weights_lo(dve, SPLIT_SLOT[j], raw_lo_vector)

            dve.memset(ones[:, :], 1.0 / D).then_inc(ones_set, 1)
            dve.wait_ge(const_loaded, 48)
            dve.tensor_scalar(bias_a, tf, -1.0, 0.0, ALU.mult, ALU.min).then_inc(biases, 1)
            dve.tensor_scalar(bias_b, tf, 0.0, None, ALU.min).then_inc(biases, 1)
            dve.wait_ge(cst_tanh, 1)
            dve.wait_ge(cst_decay, 1)
            a = Run(0)
            centre(a, 0)
            clamp(0)
            rsqrt(a, 0, range(NEWTON))
            normalise(a, 0)
            clamp(1)
            sums(0, 0)
            weigh(a)
            scan(a, ea, scan_b)
            scan(a, v, scan_a)
            for k in range(KT):
                reciprocal(a, k)
            sums(0, 1)
            for k in range(KT):
                residual(a, k)
            sums(0, 2)
            centre(a, 1)
            sums(1, 0)
            sums(1, 1)
            clamp(2)
            rsqrt(a, 1, range(NEWTON))
            clamp(3)
            normalise(a, 1)
            norm_lo(a)
            for stage in range(FLYS[2]):
                sums(2, stage)
            clamp(4)
            weights_lo(dve, 4, raw_lo_vector)
            ffn(a)
            ffn(Run(1))
            run_loop(dve, ffn)
            last = Run(RUNS - 1, 1)
            ffn(last, front=False)
            hidden_hi(last, SLOTS - 1)
            for d in range(KT):
                finish(CHUNKS - 1, 1, d, down_tail, d + 1)

        @block.gpsimd
        def _(pool):
            def channel_sum(run, k):
                if k == 0:
                    pool.wait_ge(x_loaded, run.r * 16 - 16)
                elif k == 2:
                    pool.wait_ge(x1_done, run.nth(KT - 1, KT))
                else:
                    pool.wait_ge(squared, run.nth(k // 2, 2))
                pool.wait_ge(stat, run.nth(k, 4) - 1)
                src = (xin[:, :, :], eb[:, :, :], x1[:, run.par, :, :], eb[:, :, :])[k]
                pool.tensor_tensor(psum2[:, :, :], src[:, 0:2, :], src[:, 2:4, :],
                                   ALU.add).then_inc(pair_sum, 1)
                pool.wait_ge(pair_sum, run.nth(k, 4) - 8)
                pool.tensor_tensor(psum2[:, 0, :], psum2[:, 0, :], psum2[:, 1, :],
                                   ALU.add).then_inc(chan_sum, 1)

            def add_state(run, k, term, state, scanned, done):
                pool.wait_ge(scanned, run.nth(k, KT))
                t = term[:, k, run.cols].rearrange("p (b t) -> p b t", t=T)
                s = state[:, k, run.cols].rearrange("p (b t) -> p b t", t=T)
                pool.tensor_tensor(t[:, :, 1:T], t[:, :, 1:T], s[:, :, 0:T - 1], ALU.add)
                pool.tensor_tensor(t[:, :, 0:1], t[:, :, 0:1], s[:, :, 0:1],
                                   ALU.add).then_inc(done, 1)

            def quotient(run, k):
                pool.wait_ge(rec_done, run.nth(k, KT))
                pool.wait_ge(num_done, run.nth(k, KT))
                pool.tensor_tensor(bv[:, k, run.cols], bv[:, k, run.cols], eb[:, k, run.cols],
                                   ALU.mult).then_inc(y_done, 1)

            def hidden_lo(run, j):
                if not run.half or j >= HBUF:
                    pool.wait_ge(down, run.downs(j - HBUF))
                pool.wait_ge(hid_hi, run.tile(j))
                pool.tensor_tensor(hl[:, j % HBUF, run.cols], hf[:, j % 2, run.cols],
                                   hh[:, j % HBUF, run.cols], ALU.subtract).then_inc(hid_lo, 1)

            def differences(q, stage):
                butterfly(pool, q, stage, ALU.subtract, 1, fly_sub)

            def front_step(run, step):
                if step == 1 and not run.half:
                    channel_sum(run, 1)
                elif step == 6:
                    for k in range(KT):
                        add_state(run, k, eb, ea, scan_b, den_done)
                elif step == 7:
                    for k in range(KT):
                        add_state(run, k, bv, v, scan_a, num_done)
                    quotient(run, 0)
                elif 8 <= step <= 10:
                    quotient(run, step - 7)
                    if step == 10 and not run.half:
                        channel_sum(run, 2)
                elif step == 12 and not run.half:
                    channel_sum(run, 3)

            def last_lo(run, j):
                if j > 0:
                    hidden_lo(run, j - 1)
                elif not run.half or run.r > 0:
                    hidden_lo(run.previous(), SLOTS - 1)

            def ffn(run, front=True):
                for j in range(SLOTS):
                    if run.half:
                        last_lo(run, j)
                        if run.r == 0 and j < 2:
                            for stage in last_stages[j]:
                                differences(KT - 1, stage)
                        for ahead, step in front_steps(run, j):
                            front_step(ahead, step)
                        for ahead, step in front_steps(run, j + 1):
                            if step == 0 and not ahead.half:
                                channel_sum(ahead, 0)
                        if run.r == 0 and j in SPLIT_SLOT and SPLIT_SLOT[j] not in LO_ON_VECTOR:
                            weights_lo(pool, SPLIT_SLOT[j], raw_lo_pool)
                    else:
                        for ahead, step in front_steps(run, j) if front else []:
                            if step == 0:
                                channel_sum(ahead, 0)
                            front_step(ahead, step)
                        last_lo(run, j)

            a = Run(0)
            weights_lo(pool, 0, raw_lo_pool)
            weights_lo(pool, 1, raw_lo_pool)
            differences(0, 0)
            for k in range(KT):
                add_state(a, k, eb, ea, scan_b, den_done)
            for k in range(KT):
                add_state(a, k, bv, v, scan_a, num_done)
            for k in range(KT):
                quotient(a, k)
            differences(0, 1)
            differences(0, 2)
            differences(1, 0)
            differences(1, 1)
            weights_lo(pool, 2, raw_lo_pool)
            weights_lo(pool, 3, raw_lo_pool)
            for stage in range(FLYS[2]):
                differences(2, stage)
            ffn(a)
            ffn(Run(1))
            run_loop(pool, ffn)
            last = Run(RUNS - 1, 1)
            ffn(last, front=False)
            hidden_lo(last, SLOTS - 1)


def kernel(x, ctx_2048, g_xattn, g_ffn, L0_xattn_time_decay, L0_xattn_time_first,
           L0_ffn_W1, L0_ffn_W2, L0_ffn_W3):
    import concourse.bacc as bacc
    from concourse.bass_utils import run_bass_kernel_spmd

    def chunked(a):
        return np.ascontiguousarray(
            np.asarray(a).reshape(CHUNKS, TOK, KT, P).transpose(0, 3, 2, 1))

    def up_layout(w):
        return np.ascontiguousarray(
            np.asarray(w).reshape(WP, PW, KT, P).transpose(0, 3, 2, 1).reshape(WP, P, KT * PW))

    w2 = np.asarray(L0_ffn_W2).reshape(KT, P, SLOTS, P).transpose(0, 3, 2, 1).reshape(KT, P, SLOTS * P)
    per_channel = np.stack([np.asarray(L0_xattn_time_decay).reshape(KT, P).T,
                            np.asarray(L0_xattn_time_first).reshape(KT, P).T], axis=1)
    had = np.ones((1, 1), np.float32)
    while had.shape[0] < P:
        had = np.block([[had, had], [had, -had]])
    arrays = {
        "x_t": chunked(x), "ctx_t": chunked(ctx_2048), "tdf": np.ascontiguousarray(per_channel),
        "gx": np.asarray(g_xattn), "gf": np.asarray(g_ffn),
        "w1_t": up_layout(L0_ffn_W1), "w3_t": up_layout(L0_ffn_W3), "w2_t": np.ascontiguousarray(w2),
        "had_in": np.ascontiguousarray(np.stack([had, -had], axis=1)),
    }
    nc = bacc.Bacc("TRN2", target_bir_lowering=False, num_devices=1)
    args = [nc.dram_tensor(name, a.shape, F32, kind="ExternalInput").ap() for name, a in arrays.items()]
    out = nc.dram_tensor("out_t", (CHUNKS, P, KT, TOK), F32, kind="ExternalOutput").ap()
    flamingo_block(nc, *args, out)
    got = run_bass_kernel_spmd(nc, [arrays], core_ids=[0]).results[0]["out_t"]
    return np.asarray(got).transpose(0, 3, 2, 1).reshape(B, T, D)
```
